# Optimizing a Trainium2 kernel written in Bass

```python
import numpy as np
import jax
import jax.numpy as jnp

def _softmax(x, axis=-1):
    return jax.nn.softmax(x, axis=axis)

def _gelu(x):
    return jax.nn.gelu(x, approximate=True)

def _silu(x):
    return jax.nn.silu(x)

def _sigmoid(x):
    return jax.nn.sigmoid(x)

def _layernorm(x, axis=-1, eps=1e-05):
    m = jnp.mean(x, axis=axis, keepdims=True)
    v = jnp.var(x, axis=axis, keepdims=True)
    return (x - m) / jnp.sqrt(v + eps)

def _scatter_add(tgt, idx, src, axis=0):
    return tgt.at[idx].add(src)

def _segment_sum(src, seg, n):
    return jax.ops.segment_sum(src, seg, n)
kernel_name = 'mk_gnn_resnorm_d2_gnn_r8_19bd47'

def setup_inputs(seed: int=0):
    np.random.seed(seed)
    _w = jnp.asarray

    def _rec_inputs():
        import jax
        import jax.numpy as jnp
        _gk = jax.random.key(seed)
        x = -0.000202 + 1 * jax.random.normal(jax.random.fold_in(_gk, 1), (12500, 64), jnp.float32)
        src = jax.random.randint(jax.random.fold_in(_gk, 2), (200000,), 0, 12500, jnp.int32)
        dst = jax.random.randint(jax.random.fold_in(_gk, 3), (200000,), 0, 12500, jnp.int32)
        _o = jnp.argsort(dst, stable=True)
        src = src[_o]
        dst = dst[_o]
        return (x, src, dst)
    x, src, dst = _rec_inputs()

    def _L0_gnn_setup():
        import jax, jax.numpy as jnp
        import numpy as np
        N_NODES = 12500
        N_EDGES = 200000
        D = 64
        NEG_SLOPE = 0.3

        def _gcn_norm(edge_index, num_nodes):
            loop = jnp.arange(num_nodes, dtype=edge_index.dtype)
            src = jnp.concatenate([edge_index[0], loop])
            dst = jnp.concatenate([edge_index[1], loop])
            deg = jax.ops.segment_sum(jnp.ones_like(dst, dtype=jnp.float32), dst, num_segments=num_nodes)
            dinv = jnp.where(deg > 0, jax.lax.rsqrt(deg), 0.0)
            norm = dinv[src] * dinv[dst]
            return (src, dst, norm)

        def _gcn_conv(x, W, src, dst, norm, num_nodes):
            h = x @ W
            msg = h[src] * norm[:, None]
            return jax.ops.segment_sum(msg, dst, num_segments=num_nodes)
        key = jax.random.key(seed)
        k1, k2, k3, k4 = jax.random.split(key, 4)
        x = jax.random.normal(k1, (N_NODES, D), dtype=jnp.float32)
        edge_index = jax.random.randint(k2, (2, N_EDGES), 0, N_NODES, dtype=jnp.int64)
        s = 1.0 / np.sqrt(D)
        W1 = jax.random.normal(k3, (D, D), dtype=jnp.float32) * s
        W2 = jax.random.normal(k4, (D, D), dtype=jnp.float32) * s
        return {'x': x, 'edge_index': edge_index, 'W1': W1, 'W2': W2}
    _L0_gnn_all = _L0_gnn_setup()
    _L0_gnn_in = {k: v for k, v in _L0_gnn_all.items() if k in ('W1', 'W2')}
    del _L0_gnn_all

    def _L1_gnn_setup():
        import jax, jax.numpy as jnp
        import numpy as np
        N_NODES = 12500
        N_EDGES = 200000
        IN_DIM = 64
        OUT_DIM = 64
        FLAT = IN_DIM * OUT_DIM

        def _gru_cell(inp, hid, w_ih, w_hh, b_ih, b_hh):
            gi = w_ih @ inp + b_ih
            gh = w_hh @ hid + b_hh
            i_r, i_z, i_n = jnp.split(gi, 3)
            h_r, h_z, h_n = jnp.split(gh, 3)
            r = jax.nn.sigmoid(i_r + h_r)
            z = jax.nn.sigmoid(i_z + h_z)
            n = jnp.tanh(i_n + r * h_n)
            return (1.0 - z) * n + z * hid
        key = jax.random.key(seed)
        ks = jax.random.split(key, 8)
        x = jax.random.normal(ks[0], (N_NODES, IN_DIM), dtype=jnp.float32)
        row = jax.random.randint(ks[1], (N_EDGES,), 0, N_NODES)
        offs = jax.random.randint(ks[2], (N_EDGES,), 1, N_NODES)
        col = (row + offs) % N_NODES
        edge_index = jnp.stack([row, col]).astype(jnp.int64)
        limit = float(np.sqrt(6.0 / (IN_DIM + OUT_DIM)))
        initial_weight = jax.random.uniform(ks[3], (IN_DIM, OUT_DIM), jnp.float32, -limit, limit)
        s = 1.0 / np.sqrt(FLAT)
        w_ih = jax.random.uniform(ks[4], (3 * FLAT, FLAT), jnp.float32, -s, s)
        w_hh = jax.random.uniform(ks[5], (3 * FLAT, FLAT), jnp.float32, -s, s)
        b_ih = jax.random.uniform(ks[6], (3 * FLAT,), jnp.float32, -s, s)
        b_hh = jax.random.uniform(ks[7], (3 * FLAT,), jnp.float32, -s, s)
        return {'x': x, 'edge_index': edge_index, 'initial_weight': initial_weight, 'w_ih': w_ih, 'w_hh': w_hh, 'b_ih': b_ih, 'b_hh': b_hh}
    _L1_gnn_all = _L1_gnn_setup()
    _L1_gnn_in = {k: v for k, v in _L1_gnn_all.items() if k in ('initial_weight', 'w_ih', 'w_hh', 'b_ih', 'b_hh')}
    del _L1_gnn_all
    return {'x': x, 'src': src, 'dst': dst, 'L0_gnn_W1': _L0_gnn_in['W1'], 'L0_gnn_W2': _L0_gnn_in['W2'], 'L1_gnn_initial_weight': _L1_gnn_in['initial_weight'], 'L1_gnn_w_ih': _L1_gnn_in['w_ih'], 'L1_gnn_w_hh': _L1_gnn_in['w_hh'], 'L1_gnn_b_ih': _L1_gnn_in['b_ih'], 'L1_gnn_b_hh': _L1_gnn_in['b_hh']}

def reference(x, src, dst, L0_gnn_W1, L0_gnn_W2, L1_gnn_initial_weight, L1_gnn_w_ih, L1_gnn_w_hh, L1_gnn_b_ih, L1_gnn_b_hh):
    import jax
    import jax.numpy as jnp

    def _L0_gnn_ref(x, edge_index, W1, W2):
        import jax, jax.numpy as jnp
        import numpy as np
        N_NODES = 12500
        N_EDGES = 200000
        D = 64
        NEG_SLOPE = 0.3

        def _gcn_norm(edge_index, num_nodes):
            loop = jnp.arange(num_nodes, dtype=edge_index.dtype)
            src = jnp.concatenate([edge_index[0], loop])
            dst = jnp.concatenate([edge_index[1], loop])
            deg = jax.ops.segment_sum(jnp.ones_like(dst, dtype=jnp.float32), dst, num_segments=num_nodes)
            dinv = jnp.where(deg > 0, jax.lax.rsqrt(deg), 0.0)
            norm = dinv[src] * dinv[dst]
            return (src, dst, norm)

        def _gcn_conv(x, W, src, dst, norm, num_nodes):
            h = x @ W
            msg = h[src] * norm[:, None]
            return jax.ops.segment_sum(msg, dst, num_segments=num_nodes)
        n = x.shape[0]
        src, dst, norm = _gcn_norm(edge_index, n)
        h = jax.nn.leaky_relu(_gcn_conv(x, W1, src, dst, norm, n), NEG_SLOPE)
        h = jax.nn.leaky_relu(_gcn_conv(h, W2, src, dst, norm, n), NEG_SLOPE)
        return jax.nn.relu(h)

    def _L1_gnn_ref(x, edge_index, initial_weight, w_ih, w_hh, b_ih, b_hh):
        import jax, jax.numpy as jnp
        import numpy as np
        N_NODES = 12500
        N_EDGES = 200000
        IN_DIM = 64
        OUT_DIM = 64
        FLAT = IN_DIM * OUT_DIM

        def _gru_cell(inp, hid, w_ih, w_hh, b_ih, b_hh):
            gi = w_ih @ inp + b_ih
            gh = w_hh @ hid + b_hh
            i_r, i_z, i_n = jnp.split(gi, 3)
            h_r, h_z, h_n = jnp.split(gh, 3)
            r = jax.nn.sigmoid(i_r + h_r)
            z = jax.nn.sigmoid(i_z + h_z)
            n = jnp.tanh(i_n + r * h_n)
            return (1.0 - z) * n + z * hid
        num_nodes = x.shape[0]
        in_dim, out_dim = initial_weight.shape
        h = initial_weight.reshape(-1)
        weight = _gru_cell(h, h, w_ih, w_hh, b_ih, b_hh).reshape(in_dim, out_dim)
        loop = jnp.arange(num_nodes, dtype=edge_index.dtype)
        row = jnp.concatenate([edge_index[0], loop])
        col = jnp.concatenate([edge_index[1], loop])
        deg = jax.ops.segment_sum(jnp.ones_like(col, dtype=x.dtype), col, num_segments=num_nodes)
        dis = jnp.where(deg > 0, jax.lax.rsqrt(jnp.maximum(deg, 1.0)), 0.0)
        norm = dis[row] * dis[col]
        xw = x @ weight
        msg = xw[row] * norm[:, None]
        out = jax.ops.segment_sum(msg, col, num_segments=num_nodes)
        return jax.nn.relu(out)
    edge_index = jnp.stack([src, dst])
    x = _layernorm(x + _L0_gnn_ref(x, edge_index, L0_gnn_W1, L0_gnn_W2), axis=-1)
    x = _layernorm(x + _L1_gnn_ref(x, edge_index, L1_gnn_initial_weight, L1_gnn_w_ih, L1_gnn_w_hh, L1_gnn_b_ih, L1_gnn_b_hh), axis=-1)
    return x

_drawn_inputs = setup_inputs


def setup_inputs(seed=0):
    import zlib

    import numpy as np

    out = dict(_drawn_inputs(seed))
    spreads = {}
    factors = {'L1_gnn_b_ih': 8.0, 'L1_gnn_b_hh': 8.0}
    for name, (base, spread) in spreads.items():
        noise = np.random.default_rng([zlib.crc32(name.encode()), seed]).standard_normal(out[name].shape)
        drawn = base * np.exp(spread * noise) if base else spread * noise
        out[name] = jnp.asarray(drawn.astype(out[name].dtype))
    for name, factor in factors.items():
        out[name] = (out[name] * factor).astype(out[name].dtype)
    return out
```

```python
from contextlib import ExitStack

import concourse.bass as bass
from concourse import mybir

ALU = mybir.AluOpType
ACT = mybir.ActivationFunctionType
F32 = mybir.dt.float32
BF16 = mybir.dt.bfloat16
I32 = mybir.dt.int32
AX_X = mybir.AxisListType.X

P = 128
GROUP = 8
GROUPS = 4
STEP = GROUP * GROUPS
SLOPE = 0.3
EPS = 1e-5
PIECES = 4
BANK = 512


def up(a, b):
    return -(-a // b)


def gnn_kernel(nc, x, src, dst, W1, W2, hid0, w_ih, w_hh, b_ih, b_hh, out):
    N, D = x.shape
    E = src.shape[0]
    FLAT = w_ih.shape[1]
    TILES = up(E, P)
    BLOCKS = up(N, P)
    PAIRS = TILES + BLOCKS - 1
    STEPS = up(PAIRS, STEP)
    KP = STEPS * STEP
    CH = up(TILES, P)
    PAD_DST = P * 120
    assert KP % (4 * 2) == 0 and KP // 4 <= BANK and PAD_DST // P > KP // P * 0 + BLOCKS + STEP // 8
    assert TILES + PAD_DST // P >= KP and BLOCKS <= P and D == 64
    HALF = KP // 2
    QUART = KP // 4
    FULL_T = E // P
    REST_E = E - FULL_T * P
    LAST_T = FULL_T - (CH - 1) * P
    FULL_B = N // P
    REST_N = N - FULL_B * P
    HCH = FLAT // P
    WCH = 3 * HCH
    GRU_STEPS = WCH // 2
    assert GRU_STEPS <= STEPS
    BG = 8
    BGROUPS = [(b, min(BG, BLOCKS - b)) for b in range(0, BLOCKS, BG)]
    PIECE = FLAT // PIECES

    tables = [nc.dram_tensor(f"table_{i}", (P * P, D), F32).ap() for i in range(3)]
    evolved_dram = nc.dram_tensor("evolved_weight", (HCH, P), F32).ap()

    with ExitStack() as life:
        def sem(name):
            return life.enter_context(nc.semaphore(name))

        def sb(stack, name, shape, dt):
            return stack.enter_context(nc.sbuf_tensor(name, shape, dt))

        def ps(stack, name, shape, dt=F32):
            return stack.enter_context(nc.psum_tensor(name, shape, dt))

        feats = sb(life, "feats", [P, BLOCKS, D], F32)
        table = sb(life, "table", [P, BLOCKS, D], F32)
        rel = sb(life, "rel", [P, KP + GROUP], F32)
        rows = sb(life, "rows", [P, KP], I32)
        block_col = sb(life, "block_col", [1, KP], I32)
        block_f = sb(life, "block_f", [1, KP], F32)
        ident = sb(life, "ident", [P, P], F32)
        identb = sb(life, "identb", [P, P], BF16)
        iota_n = sb(life, "iota_n", [P, P], F32)
        onesb = sb(life, "onesb", [P, P], BF16)
        onesf = sb(life, "onesf", [1, 1], F32)
        dinv = sb(life, "dinv", [P, BLOCKS], F32)
        dinv2 = sb(life, "dinv2", [P, BLOCKS], F32)
        W1s = sb(life, "W1s", [D, D], F32)
        W2s = sb(life, "W2s", [D, D], F32)
        W3s = sb(life, "W3s", [D, D], F32)
        gates_i = sb(life, "gates_i", [P, WCH], F32)
        gates_h = sb(life, "gates_h", [P, WCH], F32)

        with ExitStack() as tmp:
            edges = {}
            for name in ("dst", "src"):
                for at in ("cur", "prev"):
                    edges[name, at] = sb(tmp, f"{name}_{at}", [P, CH, P], I32)
            high = {k: sb(tmp, f"high_{k[0]}_{k[1]}", [P, CH, P], I32) for k in edges}
            low = {k: sb(tmp, f"low_{k[0]}_{k[1]}", [P, CH, P], I32) for k in edges}
            dhigh = sb(tmp, "dhigh", [P, CH, P], F32)
            dlow = sb(tmp, "dlow", [P, CH, P], F32)
            rel_hi = sb(tmp, "rel_hi", [P, CH, P], BF16)
            rel_lo = sb(tmp, "rel_lo", [P, CH, P], BF16)
            row_hi = sb(tmp, "row_hi", [P, CH, P], BF16)
            row_lo = sb(tmp, "row_lo", [P, CH, P], BF16)
            tile_no = sb(tmp, "tile_no", [P, CH], F32)
            first_pair = sb(tmp, "first_pair", [P, CH], F32)
            pair_no = sb(tmp, "pair_no", [P, KP], F32)
            minus_pair = sb(tmp, "minus_pair", [P, KP], F32)
            begun = sb(tmp, "begun", [P, 2, HALF], BF16)
            row_t = sb(tmp, "row_t", [1, KP], F32)

            rel_ps = [ps(tmp, f"rel_ps{i}", [P, BANK]) for i in range(2)]
            row_ps = [ps(tmp, f"row_ps{i}", [P, BANK]) for i in range(2)]
            cnt_ps = [ps(tmp, f"cnt_ps{i}", [1, BANK]) for i in range(2)]

            pads_set = sem("pads_set")
            edges_in = sem("edges_in")
            consts_in = sem("consts_in")
            iotas_set = sem("iotas_set")
            consts_set = sem("consts_set")
            halves = sem("halves")
            deltas = sem("deltas")
            parts_ready = sem("parts_ready")
            pairs_set = sem("pairs_set")
            begun_set = sem("begun_set")
            begun_used = sem("begun_used")
            pair_sums = sem("pair_sums")
            sums_out = sem("sums_out")
            rows_out = sem("rows_out")
            col_steps = sem("col_steps")

            block = tmp.enter_context(nc.Block())

            @block.sync
            def _(sp):
                sp.dma_start(feats[:, 0:FULL_B, :], x[0:FULL_B * P].rearrange("(b p) f -> p b f", p=P)).then_inc(consts_in, 16)
                sp.dma_start(W1s[:, :], W1[:, :]).then_inc(consts_in, 16)
                sp.dma_start(W2s[:, :], W2[:, :]).then_inc(consts_in, 16)
                sp.wait_ge(pads_set, 3)
                sp.dma_start(feats[0:REST_N, FULL_B, :], x[FULL_B * P:N]).then_inc(consts_in, 16)
                sp.wait_ge(consts_in, 64)

            @block.scalar
            def _(act):
                act.wait_ge(pads_set, 2)
                for name, arr in (("dst", dst), ("src", src)):
                    cur, prev = edges[name, "cur"], edges[name, "prev"]
                    act.dma_start(cur[:, 0:CH - 1, :], arr[0:(CH - 1) * P * P].rearrange("(c p e) -> p c e", p=P, e=P)).then_inc(edges_in, 16)
                    act.dma_start(cur[0:LAST_T, CH - 1, :], arr[(CH - 1) * P * P:FULL_T * P].rearrange("(p e) -> p e", e=P)).then_inc(edges_in, 16)
                    act.dma_start(cur[LAST_T:LAST_T + 1, CH - 1, 0:REST_E], arr[FULL_T * P:E].rearrange("(p e) -> p e", p=1)).then_inc(edges_in, 16)
                    act.dma_start(prev[1:P, 0, :], arr[0:(P - 1) * P].rearrange("(p e) -> p e", e=P)).then_inc(edges_in, 16)
                    act.dma_start(prev[:, 1:CH - 1, :], arr[(P - 1) * P:(P - 1) * P + (CH - 2) * P * P].rearrange("(c p e) -> p c e", p=P, e=P)).then_inc(edges_in, 16)
                    act.dma_start(prev[0:LAST_T + 1, CH - 1, :], arr[((CH - 1) * P - 1) * P:FULL_T * P].rearrange("(p e) -> p e", e=P)).then_inc(edges_in, 16)
                for h in range(2):
                    act.wait_ge(pair_sums, h + 1)
                    for q in range(2):
                        k = h * HALF + q * QUART
                        act.activation(rows[:, k:k + QUART], row_ps[q][:, 0:QUART], ACT.Copy).then_inc(rows_out, 1)

            @block.gpsimd
            def _(pool):
                for name, pad in (("dst", PAD_DST), ("src", 0)):
                    pool.memset(edges[name, "cur"][:, CH - 1, :], pad)
                    pool.memset(edges[name, "prev"][:, CH - 1, :], 0)
                    pool.memset(edges[name, "prev"][0:1, 0, :], 0).then_inc(pads_set, 1)
                pool.memset(feats[:, FULL_B, :], 0.0).then_inc(pads_set, 1)
                pool.iota(pair_no[:, :], [[1, KP]], base=0, channel_multiplier=0, allow_small_or_imprecise_dtypes=True).then_inc(iotas_set, 1)
                pool.iota(tile_no[:, :], [[P, CH]], base=0, channel_multiplier=1, allow_small_or_imprecise_dtypes=True).then_inc(iotas_set, 1)
                pool.iota(iota_n[:, :], [[1, P]], base=0, channel_multiplier=0, allow_small_or_imprecise_dtypes=True).then_inc(iotas_set, 1)
                pool.memset(ident[:, :], 1.0).then_inc(iotas_set, 1)
                pool.memset(onesb[:, :], 1.0).then_inc(consts_set, 1)
                pool.memset(onesf[:, :], 1.0).then_inc(consts_set, 1)
                pool.memset(rel[:, KP:KP + GROUP], -1.0).then_inc(consts_set, 1)
                pool.wait_ge(iotas_set, 4)
                pool.affine_select(ident[:, :], ident[:, :], pattern=[[1, P]], compare_op=ALU.is_equal, fill=0.0, base=0, channel_multiplier=-1).then_inc(iotas_set, 1)
                pool.wait_ge(iotas_set, 5)
                pool.tensor_copy(identb[:, :], ident[:, :]).then_inc(consts_set, 1)

            @block.tensor
            def _(pe):
                pe.wait_ge(consts_set, 2)
                pe.wait_ge(parts_ready, 4)
                for h in range(2):
                    if h == 1:
                        pe.wait_ge(sums_out, 4)
                        pe.wait_ge(rows_out, 2)
                    for c in range(CH):
                        pe.wait_ge(begun_set, h * CH + c + 1)
                        b = (h * CH + c) % 2
                        for q in range(2):
                            mask = begun[:, b, q * QUART:(q + 1) * QUART]
                            pe.matmul(rel_ps[q][:, 0:QUART], rel_hi[:, c, :], mask, start=(c == 0), stop=False)
                            pe.matmul(rel_ps[q][:, 0:QUART], rel_lo[:, c, :], mask, start=False, stop=(c == CH - 1))
                            pe.matmul(row_ps[q][:, 0:QUART], row_hi[:, c, :], mask, start=(c == 0), stop=False)
                            pe.matmul(row_ps[q][:, 0:QUART], row_lo[:, c, :], mask, start=False, stop=(c == CH - 1))
                            mm = pe.matmul(cnt_ps[q][:, 0:QUART], onesb[:, 0:1], mask, start=(c == 0), stop=(c == CH - 1))
                        mm.then_inc(begun_used, 1)
                    pe.wait_ge(begun_used, (h + 1) * CH)
                    pe.sem_inc(pair_sums, 1)

            @block.vector
            def _(dve):
                dve.wait_ge(edges_in, 16 * 12)
                for k in edges:
                    dve.tensor_scalar(high[k][:, :, :], edges[k][:, :, :], 7, None, ALU.logical_shift_right)
                    dve.tensor_scalar(low[k][:, :, :], edges[k][:, :, :], P - 1, None, ALU.bitwise_and).then_inc(halves, 1)
                dve.wait_ge(halves, 4)
                dve.tensor_tensor(dhigh[:, :, :], high["dst", "cur"][:, :, :], high["dst", "prev"][:, :, :], ALU.subtract).then_inc(deltas, 1)
                dve.tensor_tensor(rel_lo[:, :, :], low["dst", "cur"][:, :, :], low["dst", "prev"][:, :, :], ALU.subtract).then_inc(parts_ready, 1)
                dve.tensor_tensor(dlow[:, :, :], low["src", "cur"][:, :, :], low["src", "prev"][:, :, :], ALU.subtract).then_inc(deltas, 1)
                dve.tensor_tensor(row_lo[:, :, :], high["src", "cur"][:, :, :], high["src", "prev"][:, :, :], ALU.subtract).then_inc(parts_ready, 1)
                dve.wait_ge(deltas, 2)
                dve.tensor_scalar(rel_hi[:, :, :], dhigh[:, :, :], float(P), float(P), ALU.mult, ALU.add).then_inc(parts_ready, 1)
                dve.tensor_scalar(row_hi[:, :, :], dlow[:, :, :], float(P), None, ALU.mult).then_inc(parts_ready, 1)
                dve.wait_ge(iotas_set, 3)
                dve.tensor_tensor(first_pair[:, :], tile_no[:, :], high["dst", "cur"][:, :, 0], ALU.add).then_inc(pairs_set, 1)
                dve.tensor_scalar(minus_pair[:, :], pair_no[:, :], -float(P), -float(P), ALU.mult, ALU.add).then_inc(pairs_set, 1)
                dve.wait_ge(pairs_set, 2)
                dve.memset(first_pair[0:1, 0:1], 0.0).then_inc(pairs_set, 1)
                dve.wait_ge(pairs_set, 3)
                for h in range(2):
                    for c in range(CH):
                        n = h * CH + c
                        if n >= 2:
                            dve.wait_ge(begun_used, n - 1)
                        dve.tensor_scalar(begun[:, n % 2, :], pair_no[:, h * HALF:(h + 1) * HALF], first_pair[:, c:c + 1], None, ALU.is_ge).then_inc(begun_set, 1)
                    dve.wait_ge(pair_sums, h + 1)
                    for q in range(2):
                        k = h * HALF + q * QUART
                        dve.tensor_tensor(rel[:, k:k + QUART], rel_ps[q][:, 0:QUART], minus_pair[:, k:k + QUART], ALU.add).then_inc(sums_out, 1)
                        dve.tensor_tensor(row_t[:, k:k + QUART], pair_no[0:1, k:k + QUART], cnt_ps[q][:, 0:QUART], ALU.subtract).then_inc(sums_out, 1)
                dve.wait_ge(sums_out, 8)
                dve.tensor_scalar(block_f[:, :], row_t[:, :], 1.0, None, ALU.add).then_inc(col_steps, 1)
                dve.wait_ge(col_steps, 1)
                dve.tensor_scalar(row_t[:, :], block_f[:, :], float(BLOCKS - 1), float(P), ALU.min, ALU.mult).then_inc(col_steps, 1)
                dve.wait_ge(col_steps, 2)
                dve.tensor_copy(block_col[:, :], row_t[:, :]).then_inc(col_steps, 1)

        with ExitStack() as tmp:
            iota_b = sb(tmp, "iota_b", [P, P], BF16)
            zeros = sb(tmp, "zeros", [P, P - BLOCKS, D], F32)
            rel_st = sb(tmp, "rel_st", [P, 2, STEP // 2], F32)
            hot = sb(tmp, "hot", [P, 2, STEP // 2, P], BF16)
            counts = sb(tmp, "counts", [P, KP], BF16)
            counts_t = sb(tmp, "counts_t", [P, CHK := KP // P, P], BF16)
            block_of = sb(tmp, "block_of", [P, CHK], F32)
            chosen = sb(tmp, "chosen", [P, CHK, BLOCKS], BF16)
            deg = sb(tmp, "deg", [P, BLOCKS], F32)
            root = sb(tmp, "root", [P, BLOCKS], F32)
            inv0 = sb(tmp, "inv0", [P, BLOCKS], F32)
            corr = sb(tmp, "corr", [P, BLOCKS], F32)
            corr2 = sb(tmp, "corr2", [P, BLOCKS], F32)
            cnt2 = [ps(tmp, f"cnt2_{i}", [P, STEP // 2]) for i in range(2)]
            turn = [ps(tmp, f"turn{i}", [P, P], BF16) for i in range(2)]
            col_ps = ps(tmp, "col_ps", [P, CHK])
            deg_ps = ps(tmp, "deg_ps", [P, BLOCKS])

            iota_done = sem("iota_done")
            zeros_set = sem("zeros_set")
            staged = [sem(f"rel_staged{i}") for i in range(2)]
            hot_set = [sem(f"hot_set{i}") for i in range(2)]
            counted = [sem(f"counted{i}") for i in range(2)]
            counts_out = [sem(f"counts_out{i}") for i in range(2)]
            turned = sem("turned")
            turn_out = sem("turn_out")
            cols_ready = sem("cols_ready")
            cols_out = sem("cols_out")
            chosen_set = sem("chosen_set")
            deg_ready = sem("deg_ready")
            deg_steps = sem("deg_steps")
            root_done = sem("root_done")
            table_set = sem("table_set")
            table_out = sem("table_out")

            block = tmp.enter_context(nc.Block())

            @block.vector
            def _(dve):
                for b in range(2):
                    dve.sem_inc(hot_set[b], 1)
                dve.tensor_copy(iota_b[:, :], iota_n[:, :]).then_inc(iota_done, 1)
                dve.wait_ge(iota_done, 1)
                with dve.Fori(0, STEPS) as i:
                    for b in range(2):
                        dve.wait_ge(staged[b], i + 1)
                        dve.wait_ge(counted[b], i + 1)
                        for j in range(STEP // 2):
                            op = dve.tensor_scalar(hot[:, b, j, :], iota_b[:, :], rel_st[:, b, j:j + 1], None, ALU.is_equal)
                        op.then_inc(hot_set[b], 1)
                dve.wait_ge(cols_ready, 1)
                dve.tensor_copy(block_of[:, :], col_ps[:, :]).then_inc(cols_out, 1)
                dve.wait_ge(cols_out, 1)
                for c in range(CHK):
                    dve.tensor_scalar(chosen[:, c, :], iota_n[:, 0:BLOCKS], block_of[:, c:c + 1], None, ALU.is_equal).then_inc(chosen_set, 1)
                dve.wait_ge(deg_ready, 1)
                dve.tensor_scalar(deg[:, :], deg_ps[:, :], 1.0, None, ALU.add).then_inc(deg_steps, 1)
                dve.wait_ge(root_done, 1)
                dve.reciprocal(inv0[:, :], root[:, :]).then_inc(deg_steps, 1)
                dve.wait_ge(deg_steps, 2)
                dve.tensor_tensor(corr[:, :], inv0[:, :], inv0[:, :], ALU.mult).then_inc(deg_steps, 1)
                dve.wait_ge(deg_steps, 3)
                dve.tensor_tensor(corr2[:, :], corr[:, :], deg[:, :], ALU.mult).then_inc(deg_steps, 1)
                dve.wait_ge(deg_steps, 4)
                dve.tensor_scalar(corr[:, :], corr2[:, :], -0.5, 1.5, ALU.mult, ALU.add).then_inc(deg_steps, 1)
                dve.wait_ge(deg_steps, 5)
                dve.tensor_tensor(dinv[:, :], corr[:, :], inv0[:, :], ALU.mult).then_inc(deg_steps, 1)
                dve.wait_ge(deg_steps, 6)
                dve.tensor_tensor(dinv2[:, :], dinv[:, :], dinv[:, :], ALU.mult).then_inc(deg_steps, 1)
                for b, n in BGROUPS:
                    dve.tensor_tensor(table[:, b:b + n, :], feats[:, b:b + n, :], dinv[:, b:b + n].unsqueeze(2).to_broadcast([P, n, D]), ALU.mult).then_inc(table_set, 1)

            @block.tensor
            def _(pe):
                for b in range(2):
                    pe.sem_inc(counted[b], 1)
                with pe.Fori(0, STEPS) as i:
                    for b in range(2):
                        pe.wait_ge(hot_set[b], i + 2)
                        pe.wait_ge(counts_out[b], i + 1)
                        for j in range(STEP // 2):
                            mm = pe.matmul(cnt2[b][:, j:j + 1], hot[:, b, j, :], onesb[:, 0:1], start=True, stop=True)
                        mm.then_inc(counted[b], 1)
                for c in range(CHK):
                    mm = pe.matmul(col_ps[:, c:c + 1], block_f[0:1, c * P:(c + 1) * P], onesf[0:1, 0:1], start=True, stop=True)
                mm.then_inc(cols_ready, 1)
                for b in range(2):
                    pe.wait_ge(counts_out[b], STEPS + 1)
                for c in range(CHK):
                    if c >= 2:
                        pe.wait_ge(turn_out, c - 1)
                    pe.transpose(turn[c % 2][:, :], counts[:, c * P:(c + 1) * P], identb[:, :]).then_inc(turned, 1)
                pe.wait_ge(turn_out, CHK)
                pe.wait_ge(chosen_set, CHK)
                for c in range(CHK):
                    mm = pe.matmul(deg_ps[:, :], counts_t[:, c, :], chosen[:, c, :], start=(c == 0), stop=(c == CHK - 1))
                mm.then_inc(deg_ready, 1)

            @block.scalar
            def _(act):
                H = STEP // 2
                for b in range(2):
                    act.sem_inc(counts_out[b], 1)
                with act.Fori(0, STEPS) as i:
                    for b in range(2):
                        act.wait_ge(hot_set[b], i + 1)
                        act.activation(rel_st[:, b, :], rel[:, bass.ds(i * STEP + b * H, H)], ACT.Copy).then_inc(staged[b], 1)
                    for b in range(2):
                        act.wait_ge(counted[b], i + 2)
                        act.activation(counts[:, bass.ds(i * STEP + b * H, H)], cnt2[b][:, :], ACT.Copy).then_inc(counts_out[b], 1)
                for c in range(CHK):
                    act.wait_ge(turned, c + 1)
                    act.activation(counts_t[:, c, :], turn[c % 2][:, :], ACT.Copy).then_inc(turn_out, 1)
                act.wait_ge(deg_steps, 1)
                act.activation(root[:, :], deg[:, :], ACT.Sqrt).then_inc(root_done, 1)

            @block.gpsimd
            def _(pool):
                pool.memset(zeros[:, :, :], 0.0).then_inc(zeros_set, 1)

            @block.sync
            def _(sp):
                sp.wait_ge(zeros_set, 1)
                for t in tables:
                    sp.dma_start(t.rearrange("(p s) f -> p s f", p=P)[:, BLOCKS:P, :], zeros[:, :, :]).then_inc(table_out, 16)
                for g, (b, n) in enumerate(BGROUPS):
                    sp.wait_ge(table_set, g + 1)
                    sp.dma_start(tables[0].rearrange("(p s) f -> p s f", p=P)[:, b:b + n, :], table[:, b:b + n, :]).then_inc(table_out, 16)
                sp.wait_ge(table_out, 16 * (len(BGROUPS) + len(tables)))

        sums = sb(life, "sums", [D, BLOCKS * P], F32)

        def convolve(no, gru):
            with ExitStack() as tmp:
                row_st = sb(tmp, f"row_st_{no}", [P, 2, STEP // 2], I32)
                msgs = sb(tmp, f"msgs_{no}", [P, STEP, D], F32)
                hot = sb(tmp, f"hot_{no}", [P, 2, GROUP, P], F32)
                if gru:
                    wbuf = [sb(tmp, f"wbuf{i}_{no}", [P, FLAT], F32) for i in range(2)]
                    hidden = sb(tmp, f"hidden_{no}", [P, FLAT], F32)
                    partial = sb(tmp, f"partial_{no}", [P, 2, PIECES], F32)
                pair_ps = [ps(tmp, f"pair_ps{i}_{no}", [D, GROUP, P]) for i in range(2)]
                iota_ps = ps(tmp, f"iota_ps_{no}", [P, BANK])
                turn = [ps(tmp, f"turn{i}_{no}", [D, 4 * P]) for i in range(2)]

                hidden_in = sem(f"hidden_in_{no}")
                turned = sem(f"turned_{no}")
                turn_out = sem(f"turn_out_{no}")
                rows_staged = [sem(f"rows_staged{i}_{no}") for i in range(2)]
                group_opened = sem(f"group_opened_{no}")
                landed = [sem(f"landed{i}_{no}") for i in range(GROUPS)]
                hot_set = [sem(f"hot_set{i}_{no}") for i in range(2)]
                multiplied = [sem(f"multiplied{i}_{no}") for i in range(GROUPS)]
                added = sem(f"added_{no}")
                added_group = [sem(f"added_group{i}_{no}") for i in range(2)]
                iota_set = sem(f"iota_set_{no}")
                w_used_parts = sem(f"w_used_parts_{no}")
                w_in = [sem(f"w_in{i}_{no}") for i in range(2)]
                w_used = [sem(f"w_used{i}_{no}") for i in range(2)]
                TURNS = [(b, min(4, BLOCKS - b)) for b in range(0, BLOCKS, 4)]
                H = STEP // 2

                block = tmp.enter_context(nc.Block())

                @block.gpsimd
                def _(pool):
                    with pool.Fori(0, STEPS) as i:
                        for g in range(GROUPS):
                            if g % 2 == 0:
                                pool.wait_ge(rows_staged[g // 2], i + 1)
                            pool.wait_ge(multiplied[g], i + 1)
                            pool.sem_inc(group_opened, 1)
                            for j in range(GROUP):
                                s = g * GROUP + j
                                pool.indirect_dma_start(
                                    out=msgs[:, s, :], out_offset=None, in_=tables[no][:, :],
                                    in_offset=bass.IndirectOffsetOnAxis(ap=row_st[:, g // 2, s % H:s % H + 1], axis=0),
                                ).then_inc(landed[g], 16)

                @block.scalar
                def _(act):
                    def stage(i, b, first):
                        if not first:
                            act.wait_ge(landed[2 * b], i * 16 * GROUP)
                            act.wait_ge(landed[2 * b + 1], i * 16 * GROUP)
                        act.activation(row_st[:, b, :], rows[:, bass.ds(i * STEP + b * H, H)], ACT.Copy).then_inc(rows_staged[b], 1)

                    stage(0, 0, True)
                    stage(0, 1, True)
                    for n, (b, m) in enumerate(TURNS):
                        act.wait_ge(turned, n + 1)
                        act.activation(sums[:, b * P:(b + m) * P], turn[n % 2][:, 0:m * P], ACT.Copy).then_inc(turn_out, 1)
                    with act.Fori(1, STEPS) as i:
                        stage(i, 0, False)
                        stage(i, 1, False)

                @block.tensor
                def _(pe):
                    for g in range(GROUPS):
                        pe.sem_inc(multiplied[g], 1)
                    for n, (b, m) in enumerate(TURNS):
                        if n >= 2:
                            pe.wait_ge(turn_out, n - 1)
                        for j in range(m):
                            mm = pe.transpose(turn[n % 2][:, j * P:(j + 1) * P], table[:, b + j, :], ident[:, :])
                        mm.then_inc(turned, 1)
                    with pe.Fori(0, STEPS) as i:
                        for g in range(GROUPS):
                            pe.wait_ge(added_group[g % 2], 2 * i + g // 2 + 1)
                            pe.wait_ge(hot_set[g % 2], 2 * i + g // 2 + 1)
                            pe.wait_ge(landed[g], (i + 1) * (16 * GROUP))
                            for j in range(GROUP):
                                mm = pe.matmul(pair_ps[g % 2][:, j, :], msgs[:, g * GROUP + j, :], hot[:, g % 2, j, :], start=True, stop=True)
                            mm.then_inc(multiplied[g], 1)

                @block.sync
                def _(sp):
                    if gru:
                        sp.dma_start(hidden[:, :], hid0.rearrange("(o a) b -> o (a b)", o=1).to_broadcast([P, FLAT])).then_inc(hidden_in, 16)
                        with sp.Fori(0, GRU_STEPS) as i:
                            for b in range(2):
                                sp.wait_ge(w_used[b], i + 1)
                                sp.dma_start(wbuf[b][:, :], gru[0][bass.ds((2 * i + b) * P, P), :]).then_inc(w_in[b], 16)

                @block.vector
                def _(dve):
                    def build(col, b):
                        dve.tensor_tensor(
                            hot[:, b, :, :],
                            iota_ps[:, 0:P].unsqueeze(1).to_broadcast([P, GROUP, P]),
                            rel[:, bass.ds(col, GROUP)].unsqueeze(2).to_broadcast([P, GROUP, P]),
                            ALU.is_equal).then_inc(hot_set[b], 1)

                    def add(i, g):
                        _, cols = nc.values_load_multi_w_load_instructions(
                            block_col[0:1, bass.ds(i * STEP + g * GROUP, GROUP)], [mybir.EngineType.DVE],
                            min_val=0, max_val=(BLOCKS - 1) * P, 
                            skip_runtime_bounds_check_because="each is 128 times the least of a block number and BLOCKS - 1")
                        dve.wait_ge(multiplied[g], i + 2)
                        for j in range(GROUP):
                            dve.wait_ge(added, i * STEP + g * GROUP + j + 1)
                            at = sums[:, bass.ds(cols[j], P)]
                            dve.tensor_tensor(at, pair_ps[g % 2][:, j, :], at, ALU.add).then_inc(added, 1)
                        dve.wait_ge(added, i * STEP + (g + 1) * GROUP + 1)
                        dve.sem_inc(added_group[g % 2], 1)

                    def multiply(b, half):
                        for q in range(PIECES // 2 * half, PIECES // 2 * (half + 1)):
                            piece = wbuf[b][:, q * PIECE:(q + 1) * PIECE]
                            dve.tensor_tensor_reduce(piece, piece, hidden[:, q * PIECE:(q + 1) * PIECE], 1.0, 0.0, ALU.mult, ALU.add, partial[:, b, q:q + 1]).then_inc(w_used_parts, 1)

                    dve.sem_inc(added, 1)
                    for b in range(2):
                        dve.sem_inc(added_group[b], 1)
                        if gru:
                            dve.sem_inc(w_used[b], 1)
                    dve.tensor_copy(iota_ps[:, 0:P], iota_n[:, :]).then_inc(iota_set, 1)
                    dve.wait_ge(iota_set, 1)
                    build(0, 0)
                    dve.wait_ge(turn_out, len(TURNS))
                    if gru:
                        dve.wait_ge(hidden_in, 16)
                        with dve.Fori(0, GRU_STEPS) as i:
                            for g in range(GROUPS):
                                build(i * STEP + (g + 1) * GROUP, (g + 1) % 2)
                                if g % 2 == 0:
                                    dve.wait_ge(w_in[g // 2], (i + 1) * 16)
                                multiply(g // 2, g % 2)
                                add(i, g)
                                if g % 2 == 1:
                                    dve.wait_ge(w_used_parts, i * (2 * PIECES) + (g // 2 + 1) * PIECES)
                                    dve.tensor_reduce(gru[1][:, bass.ds(2 * i + g // 2, 1)], partial[:, g // 2, :], AX_X, ALU.add).then_inc(w_used[g // 2], 1)
                    with dve.Fori(GRU_STEPS if gru else 0, STEPS) as i:
                        for g in range(GROUPS):
                            build(i * STEP + (g + 1) * GROUP, (g + 1) % 2)
                            add(i, g)

        def finish(no, weight, kind):
            with ExitStack() as tmp:
                prod = [ps(tmp, f"prod{i}_{no}", [P, BG, D]) for i in range(2)]
                v = [sb(tmp, f"v{i}_{no}", [P, BG, D], F32) for i in range(2)]
                res = sb(tmp, f"res_{no}", [P, BG, D], F32)
                cen = [sb(tmp, f"cen{i}_{no}", [P, BG, D], F32) for i in range(2)]
                sq = [sb(tmp, f"sq{i}_{no}", [P, BG, D], F32) for i in range(2)]
                tot = sb(tmp, f"tot_{no}", [P, BG], F32)
                mean = sb(tmp, f"mean_{no}", [P, BG], F32)
                var = sb(tmp, f"var_{no}", [P, BG], F32)
                vare = sb(tmp, f"vare_{no}", [P, BG], F32)
                std = sb(tmp, f"std_{no}", [P, BG], F32)
                rstd = sb(tmp, f"rstd_{no}", [P, BG], F32)
                multiplied = sem(f"fin_multiplied_{no}")
                scaled = sem(f"fin_scaled_{no}")
                s = sem(f"fin_steps_{no}")
                squared = sem(f"squared_{no}")
                centred = sem(f"centred_{no}")
                var_set = sem(f"var_set_{no}")
                std_set = sem(f"std_set_{no}")
                done = sem(f"rows_done_{no}")
                stored = sem(f"stored_{no}")
                block = tmp.enter_context(nc.Block())

                @block.tensor
                def _(pe):
                    for g, (b, n) in enumerate(BGROUPS):
                        if g >= 2:
                            pe.wait_ge(scaled, g - 1)
                        for j in range(n):
                            mm = pe.matmul(prod[g % 2][:, j, :], sums[:, (b + j) * P:(b + j + 1) * P], weight[:, :], start=True, stop=True)
                        mm.then_inc(multiplied, 1)

                @block.vector
                def _(dve):
                    steps = 0

                    def step(op):
                        nonlocal steps
                        op.then_inc(s, 1)
                        steps += 1
                        dve.wait_ge(s, steps)

                    def wide(a, n):
                        return a.unsqueeze(2).to_broadcast([P, n, D])

                    for g, (b, n) in enumerate(BGROUPS):
                        scale = dinv2 if kind == "leaky" else dinv
                        vb = v[g % 2][:, 0:n, :]
                        dve.wait_ge(multiplied, g + 1)
                        dve.tensor_tensor(vb, prod[g % 2][:, 0:n, :], wide(scale[:, b:b + n], n), ALU.mult).then_inc(scaled, 1)
                        dve.wait_ge(scaled, g + 1)
                        if kind == "leaky":
                            dve.scalar_tensor_tensor(out=table[:, b:b + n, :], in0=vb, scalar=SLOPE, in1=vb, op0=ALU.mult, op1=ALU.max).then_inc(done, 1)
                            continue
                        cb, qb = cen[g % 2][:, 0:n, :], sq[g % 2][:, 0:n, :]
                        step(dve.scalar_tensor_tensor(out=res[:, 0:n, :], in0=vb, scalar=0.0, in1=feats[:, b:b + n, :], op0=ALU.max, op1=ALU.add))
                        step(dve.tensor_reduce(tot[:, 0:n], res[:, 0:n, :], AX_X, ALU.add))
                        step(dve.tensor_scalar(mean[:, 0:n], tot[:, 0:n], 1.0 / D, None, ALU.mult))
                        dve.tensor_tensor(cb, res[:, 0:n, :], wide(mean[:, 0:n], n), ALU.subtract).then_inc(centred, 1)
                        dve.wait_ge(squared, g + 1)
                        step(dve.tensor_reduce(var[:, 0:n], qb, AX_X, ALU.add))
                        dve.tensor_scalar(vare[:, 0:n], var[:, 0:n], 1.0 / D, EPS, ALU.mult, ALU.add).then_inc(var_set, 1)
                        dve.wait_ge(std_set, g + 1)
                        step(dve.reciprocal(rstd[:, 0:n], std[:, 0:n]))
                        if kind == "norm":
                            step(dve.tensor_tensor(feats[:, b:b + n, :], cb, wide(rstd[:, 0:n], n), ALU.mult))
                            dve.tensor_tensor(table[:, b:b + n, :], feats[:, b:b + n, :], wide(dinv[:, b:b + n], n), ALU.mult).then_inc(done, 1)
                        else:
                            dve.tensor_tensor(table[:, b:b + n, :], cb, wide(rstd[:, 0:n], n), ALU.mult).then_inc(done, 1)

                @block.scalar
                def _(act):
                    if kind == "leaky":
                        return
                    for g, (b, n) in enumerate(BGROUPS):
                        act.wait_ge(centred, g + 1)
                        act.activation(sq[g % 2][:, 0:n, :], cen[g % 2][:, 0:n, :], ACT.Square).then_inc(squared, 1)
                        act.wait_ge(var_set, g + 1)
                        act.activation(std[:, 0:n], vare[:, 0:n], ACT.Sqrt).then_inc(std_set, 1)

                @block.sync
                def _(sp):
                    stores = 0
                    for g, (b, n) in enumerate(BGROUPS):
                        sp.wait_ge(done, g + 1)
                        if kind != "out":
                            sp.dma_start(tables[no + 1].rearrange("(p s) f -> p s f", p=P)[:, b:b + n, :], table[:, b:b + n, :]).then_inc(stored, 16)
                            stores += 1
                            continue
                        whole = min(b + n, FULL_B) - b
                        if whole:
                            sp.dma_start(out[b * P:(b + whole) * P].rearrange("(b p) f -> p b f", p=P), table[:, b:b + whole, :]).then_inc(stored, 16)
                            stores += 1
                        if whole < n:
                            sp.dma_start(out[FULL_B * P:N], table[0:REST_N, FULL_B, :]).then_inc(stored, 16)
                            stores += 1
                    sp.wait_ge(stored, 16 * stores)

        def evolve():
            with ExitStack() as tmp:
                bias = [sb(tmp, f"bias{i}", [WCH, P], F32) for i in range(2)]
                hrow = sb(tmp, "hrow", [HCH, P], F32)
                hcol = sb(tmp, "hcol", [P, HCH], F32)
                gi = sb(tmp, "gi", [P, WCH], F32)
                gh = sb(tmp, "gh", [P, WCH], F32)
                pre = sb(tmp, "pre", [P, 2 * HCH], F32)
                gate = sb(tmp, "gate", [P, 2 * HCH], F32)
                nin = sb(tmp, "nin", [P, HCH], F32)
                nin2 = sb(tmp, "nin2", [P, HCH], F32)
                new = sb(tmp, "new", [P, HCH], F32)
                diff = sb(tmp, "diff", [P, HCH], F32)
                keep = sb(tmp, "keep", [P, HCH], F32)
                evo = sb(tmp, "evo", [P, HCH], F32)
                evo_row = sb(tmp, "evo_row", [HCH, P], F32)
                bias_ps = [ps(tmp, f"bias_ps{i}", [P, WCH]) for i in range(2)]
                h_ps = ps(tmp, "h_ps", [P, HCH])
                evo_ps = ps(tmp, "evo_ps", [HCH, P])
                loaded = sem("bias_loaded")
                turned = sem("bias_turned")
                steps = sem("gru_steps")
                act_steps = sem("gru_act_steps")
                evo_turned = sem("evo_turned")
                evo_copied = sem("evo_copied")
                stored = sem("evo_stored")
                block = tmp.enter_context(nc.Block())

                @block.sync
                def _(sp):
                    sp.dma_start(bias[0][:, :], b_ih.rearrange("(c p) -> c p", p=P)).then_inc(loaded, 16)
                    sp.dma_start(bias[1][:, :], b_hh.rearrange("(c p) -> c p", p=P)).then_inc(loaded, 16)
                    sp.dma_start(hrow[:, :], hid0.rearrange("a b -> (a b)").rearrange("(c p) -> c p", p=P)).then_inc(loaded, 16)
                    sp.wait_ge(evo_copied, 1)
                    sp.dma_start(evolved_dram[:, :], evo_row[:, :]).then_inc(stored, 16)
                    sp.wait_ge(stored, 16)
                    sp.dma_start(W3s[:, :], evolved_dram.rearrange("c p -> (c p)").rearrange("(a b) -> a b", b=D)).then_inc(stored, 16)
                    sp.wait_ge(stored, 32)

                @block.tensor
                def _(pe):
                    pe.wait_ge(loaded, 48)
                    pe.transpose(bias_ps[0][:, :], bias[0][:, :], ident[0:WCH, 0:WCH])
                    pe.transpose(bias_ps[1][:, :], bias[1][:, :], ident[0:WCH, 0:WCH])
                    pe.transpose(h_ps[:, :], hrow[:, :], ident[0:HCH, 0:HCH]).then_inc(turned, 1)
                    pe.wait_ge(steps, 8)
                    pe.transpose(evo_ps[:, :], evo[:, :], ident[:, :]).then_inc(evo_turned, 1)

                @block.vector
                def _(dve):
                    dve.wait_ge(turned, 1)
                    dve.tensor_copy(hcol[:, :], h_ps[:, :])
                    dve.tensor_tensor(gi[:, :], gates_i[:, :], bias_ps[0][:, :], ALU.add)
                    dve.tensor_tensor(gh[:, :], gates_h[:, :], bias_ps[1][:, :], ALU.add).then_inc(steps, 1)
                    dve.wait_ge(steps, 1)
                    dve.tensor_tensor(pre[:, :], gi[:, 0:2 * HCH], gh[:, 0:2 * HCH], ALU.add).then_inc(steps, 1)
                    dve.wait_ge(act_steps, 1)
                    dve.tensor_tensor(nin[:, :], gate[:, 0:HCH], gh[:, 2 * HCH:], ALU.mult).then_inc(steps, 1)
                    dve.wait_ge(steps, 3)
                    dve.tensor_tensor(nin2[:, :], nin[:, :], gi[:, 2 * HCH:], ALU.add).then_inc(steps, 1)
                    dve.wait_ge(act_steps, 2)
                    dve.tensor_tensor(keep[:, :], gate[:, HCH:], hcol[:, :], ALU.mult).then_inc(steps, 1)
                    dve.tensor_scalar(diff[:, :], gate[:, HCH:], -1.0, 1.0, ALU.mult, ALU.add).then_inc(steps, 1)
                    dve.wait_ge(steps, 6)
                    dve.tensor_tensor(nin[:, :], diff[:, :], new[:, :], ALU.mult).then_inc(steps, 1)
                    dve.wait_ge(steps, 7)
                    dve.tensor_tensor(evo[:, :], nin[:, :], keep[:, :], ALU.add).then_inc(steps, 1)
                    dve.wait_ge(evo_turned, 1)
                    dve.tensor_copy(evo_row[:, :], evo_ps[:, :]).then_inc(evo_copied, 1)

                @block.scalar
                def _(act):
                    act.wait_ge(steps, 2)
                    act.activation(gate[:, :], pre[:, :], ACT.Sigmoid).then_inc(act_steps, 1)
                    act.wait_ge(steps, 4)
                    act.activation(new[:, :], nin2[:, :], ACT.Tanh).then_inc(act_steps, 1)

        convolve(0, (w_ih, gates_i))
        finish(0, W1s, "leaky")
        convolve(1, (w_hh, gates_h))
        finish(1, W2s, "norm")
        evolve()
        convolve(2, None)
        finish(2, W3s, "out")


_INS = ["x", "src", "dst", "L0_gnn_W1", "L0_gnn_W2", "L1_gnn_initial_weight", "L1_gnn_w_ih",
        "L1_gnn_w_hh", "L1_gnn_b_ih", "L1_gnn_b_hh"]
_OUTS = [((12500, 64), "float32")]


def kernel(**inputs):
    import numpy as _np
    import concourse.bacc as _bacc
    from concourse import mybir as _mybir
    from concourse.bass_utils import run_bass_kernel_spmd as _run

    nc = _bacc.Bacc("TRN2", target_bir_lowering=False, num_devices=1)
    arrays, args = {}, []
    for name in _INS:
        a = _np.ascontiguousarray(inputs[name])
        arrays[f"in_{name}_dram"] = a
        args.append(nc.dram_tensor(f"in_{name}_dram", a.shape, _mybir.dt.from_np(a.dtype), kind="ExternalInput").ap())
    for i, (shape, dtype) in enumerate(_OUTS):
        dt = _mybir.dt.from_np(_np.dtype(dtype))
        args.append(nc.dram_tensor(f"out_{i}_dram", shape, dt, kind="ExternalOutput").ap())
    gnn_kernel(nc, *args)
    r = _run(nc, [arrays], core_ids=[0])
    return r.results[0]["out_0_dram"]
```
